# Optimizing a Trainium2 kernel written in Bass

```python
import numpy as np
import jax
import jax.numpy as jnp

def _softmax(x, axis=-1):
    return jax.nn.softmax(x, axis=axis)

def _gelu(x):
    return jax.nn.gelu(x, approximate=True)

def _silu(x):
    return jax.nn.silu(x)

def _sigmoid(x):
    return jax.nn.sigmoid(x)

def _layernorm(x, axis=-1, eps=1e-05):
    m = jnp.mean(x, axis=axis, keepdims=True)
    v = jnp.var(x, axis=axis, keepdims=True)
    return (x - m) / jnp.sqrt(v + eps)

def _scatter_add(tgt, idx, src, axis=0):
    return tgt.at[idx].add(src)

def _segment_sum(src, seg, n):
    return jax.ops.segment_sum(src, seg, n)
kernel_name = 'mk_dlrm_tower_d1_rec_r8_20a897'

def setup_inputs(seed: int=0):
    np.random.seed(seed)
    _w = jnp.asarray

    def _rec_inputs():
        import jax
        import jax.numpy as jnp
        _tk = jax.random.key(seed)
        ids = jnp.stack([jax.random.randint(jax.random.fold_in(_tk, 200 + f), (512,), 0, v, jnp.int32) for f, v in enumerate([12500, 1250, 125000, 12500, 1250, 1000, 12500, 1250, 1250, 12500, 12500, 1000, 1000, 1000, 1250, 12500, 1250, 12500, 12500, 1250, 1000, 1250, 1250, 1250, 1000, 1000])], axis=1)
        tbl_0 = 0.05 * jax.random.normal(jax.random.fold_in(_tk, 500 + 0), (12500, 128), jnp.float32)
        tbl_1 = 0.05 * jax.random.normal(jax.random.fold_in(_tk, 500 + 1), (1250, 128), jnp.float32)
        tbl_2 = 0.05 * jax.random.normal(jax.random.fold_in(_tk, 500 + 2), (125000, 128), jnp.float32)
        tbl_3 = 0.05 * jax.random.normal(jax.random.fold_in(_tk, 500 + 3), (12500, 128), jnp.float32)
        tbl_4 = 0.05 * jax.random.normal(jax.random.fold_in(_tk, 500 + 4), (1250, 128), jnp.float32)
        tbl_5 = 0.05 * jax.random.normal(jax.random.fold_in(_tk, 500 + 5), (1000, 128), jnp.float32)
        tbl_6 = 0.05 * jax.random.normal(jax.random.fold_in(_tk, 500 + 6), (12500, 128), jnp.float32)
        tbl_7 = 0.05 * jax.random.normal(jax.random.fold_in(_tk, 500 + 7), (1250, 128), jnp.float32)
        tbl_8 = 0.05 * jax.random.normal(jax.random.fold_in(_tk, 500 + 8), (1250, 128), jnp.float32)
        tbl_9 = 0.05 * jax.random.normal(jax.random.fold_in(_tk, 500 + 9), (12500, 128), jnp.float32)
        tbl_10 = 0.05 * jax.random.normal(jax.random.fold_in(_tk, 500 + 10), (12500, 128), jnp.float32)
        tbl_11 = 0.05 * jax.random.normal(jax.random.fold_in(_tk, 500 + 11), (1000, 128), jnp.float32)
        tbl_12 = 0.05 * jax.random.normal(jax.random.fold_in(_tk, 500 + 12), (1000, 128), jnp.float32)
        tbl_13 = 0.05 * jax.random.normal(jax.random.fold_in(_tk, 500 + 13), (1000, 128), jnp.float32)
        tbl_14 = 0.05 * jax.random.normal(jax.random.fold_in(_tk, 500 + 14), (1250, 128), jnp.float32)
        tbl_15 = 0.05 * jax.random.normal(jax.random.fold_in(_tk, 500 + 15), (12500, 128), jnp.float32)
        tbl_16 = 0.05 * jax.random.normal(jax.random.fold_in(_tk, 500 + 16), (1250, 128), jnp.float32)
        tbl_17 = 0.05 * jax.random.normal(jax.random.fold_in(_tk, 500 + 17), (12500, 128), jnp.float32)
        tbl_18 = 0.05 * jax.random.normal(jax.random.fold_in(_tk, 500 + 18), (12500, 128), jnp.float32)
        tbl_19 = 0.05 * jax.random.normal(jax.random.fold_in(_tk, 500 + 19), (1250, 128), jnp.float32)
        tbl_20 = 0.05 * jax.random.normal(jax.random.fold_in(_tk, 500 + 20), (1000, 128), jnp.float32)
        tbl_21 = 0.05 * jax.random.normal(jax.random.fold_in(_tk, 500 + 21), (1250, 128), jnp.float32)
        tbl_22 = 0.05 * jax.random.normal(jax.random.fold_in(_tk, 500 + 22), (1250, 128), jnp.float32)
        tbl_23 = 0.05 * jax.random.normal(jax.random.fold_in(_tk, 500 + 23), (1250, 128), jnp.float32)
        tbl_24 = 0.05 * jax.random.normal(jax.random.fold_in(_tk, 500 + 24), (1000, 128), jnp.float32)
        tbl_25 = 0.05 * jax.random.normal(jax.random.fold_in(_tk, 500 + 25), (1000, 128), jnp.float32)
        _rk = jax.random.fold_in(_tk, 7)
        r_dense_features = -0.000520686 + 1.00062 * jax.random.normal(jax.random.fold_in(_rk, 101), (512, 128), jnp.float32)
        W_top1 = 0.0405887 * jax.random.normal(jax.random.fold_in(_tk, 801), (607, 512), jnp.float32)
        W_top2 = 0.0441942 * jax.random.normal(jax.random.fold_in(_tk, 802), (512, 256), jnp.float32)
        W_top3 = 0.0625 * jax.random.normal(jax.random.fold_in(_tk, 803), (256, 1), jnp.float32)
        b_top1 = jnp.zeros((512,), jnp.float32)
        b_top2 = jnp.zeros((256,), jnp.float32)
        return (r_dense_features, ids, tbl_0, tbl_1, tbl_2, tbl_3, tbl_4, tbl_5, tbl_6, tbl_7, tbl_8, tbl_9, tbl_10, tbl_11, tbl_12, tbl_13, tbl_14, tbl_15, tbl_16, tbl_17, tbl_18, tbl_19, tbl_20, tbl_21, tbl_22, tbl_23, tbl_24, tbl_25, W_top1, b_top1, W_top2, b_top2, W_top3)
    r_dense_features, ids, tbl_0, tbl_1, tbl_2, tbl_3, tbl_4, tbl_5, tbl_6, tbl_7, tbl_8, tbl_9, tbl_10, tbl_11, tbl_12, tbl_13, tbl_14, tbl_15, tbl_16, tbl_17, tbl_18, tbl_19, tbl_20, tbl_21, tbl_22, tbl_23, tbl_24, tbl_25, W_top1, b_top1, W_top2, b_top2, W_top3 = _rec_inputs()

    def _L0_rec_setup():
        import jax, jax.numpy as jnp
        import numpy as np
        B, F, D = (2048, 26, 128)
        key = jax.random.key(seed)
        k1, k2 = jax.random.split(key)
        dense_features = jax.random.normal(k1, (B, D), dtype=jnp.float32)
        sparse_values = jax.random.normal(k2, (B, F, D), dtype=jnp.float32)
        return {'dense_features': dense_features, 'sparse_values': sparse_values}
    _L0_rec_all = _L0_rec_setup()
    _L0_rec_in = {k: v for k, v in _L0_rec_all.items() if k in ()}
    del _L0_rec_all
    return {'r_dense_features': r_dense_features, 'ids': ids, 'tbl_0': tbl_0, 'tbl_1': tbl_1, 'tbl_2': tbl_2, 'tbl_3': tbl_3, 'tbl_4': tbl_4, 'tbl_5': tbl_5, 'tbl_6': tbl_6, 'tbl_7': tbl_7, 'tbl_8': tbl_8, 'tbl_9': tbl_9, 'tbl_10': tbl_10, 'tbl_11': tbl_11, 'tbl_12': tbl_12, 'tbl_13': tbl_13, 'tbl_14': tbl_14, 'tbl_15': tbl_15, 'tbl_16': tbl_16, 'tbl_17': tbl_17, 'tbl_18': tbl_18, 'tbl_19': tbl_19, 'tbl_20': tbl_20, 'tbl_21': tbl_21, 'tbl_22': tbl_22, 'tbl_23': tbl_23, 'tbl_24': tbl_24, 'tbl_25': tbl_25, 'W_top1': W_top1, 'b_top1': b_top1, 'W_top2': W_top2, 'b_top2': b_top2, 'W_top3': W_top3}

def reference(r_dense_features, ids, tbl_0, tbl_1, tbl_2, tbl_3, tbl_4, tbl_5, tbl_6, tbl_7, tbl_8, tbl_9, tbl_10, tbl_11, tbl_12, tbl_13, tbl_14, tbl_15, tbl_16, tbl_17, tbl_18, tbl_19, tbl_20, tbl_21, tbl_22, tbl_23, tbl_24, tbl_25, W_top1, b_top1, W_top2, b_top2, W_top3):
    import jax
    import jax.numpy as jnp

    def _L0_rec_ref(dense_features, sparse_values):
        import jax, jax.numpy as jnp
        import numpy as np
        B, F, D = (2048, 26, 128)
        sd = jnp.einsum('bfd,bd->bf', sparse_values, dense_features)
        ss = jnp.einsum('bfd,bgd->bfg', sparse_values, sparse_values)
        iu, ju = jnp.triu_indices(F, k=1)
        pairs = ss[:, iu, ju]
        return jnp.concatenate([dense_features, sd, pairs], axis=1)
    e = jnp.stack([tbl_0[ids[:, 0]], tbl_1[ids[:, 1]], tbl_2[ids[:, 2]], tbl_3[ids[:, 3]], tbl_4[ids[:, 4]], tbl_5[ids[:, 5]], tbl_6[ids[:, 6]], tbl_7[ids[:, 7]], tbl_8[ids[:, 8]], tbl_9[ids[:, 9]], tbl_10[ids[:, 10]], tbl_11[ids[:, 11]], tbl_12[ids[:, 12]], tbl_13[ids[:, 13]], tbl_14[ids[:, 14]], tbl_15[ids[:, 15]], tbl_16[ids[:, 16]], tbl_17[ids[:, 17]], tbl_18[ids[:, 18]], tbl_19[ids[:, 19]], tbl_20[ids[:, 20]], tbl_21[ids[:, 21]], tbl_22[ids[:, 22]], tbl_23[ids[:, 23]], tbl_24[ids[:, 24]], tbl_25[ids[:, 25]]], axis=1)
    z = _L0_rec_ref(r_dense_features, e)
    z = z.reshape(z.shape[0], -1)
    h = jnp.concatenate([z, r_dense_features], axis=1)
    h = jnp.maximum(h @ W_top1 + b_top1, 0.0)
    h = jnp.maximum(h @ W_top2 + b_top2, 0.0)
    y = h @ W_top3
    return y

_drawn_inputs = setup_inputs


def setup_inputs(seed=0):
    import zlib

    import numpy as np

    out = dict(_drawn_inputs(seed))
    spreads = {'b_top1': (0.0, 0.1), 'b_top2': (0.0, 0.1)}
    factors = {}
    for name, (base, spread) in spreads.items():
        noise = np.random.default_rng([zlib.crc32(name.encode()), seed]).standard_normal(out[name].shape)
        drawn = base * np.exp(spread * noise) if base else spread * noise
        out[name] = jnp.asarray(drawn.astype(out[name].dtype))
    for name, factor in factors.items():
        out[name] = (out[name] * factor).astype(out[name].dtype)
    return out
```

```python
import concourse.bass as bass
from concourse import mybir
from contextlib import ExitStack

P = 128
F = 26
NF = F + 1
SLOT = 32
T = 4
SH = NF // 2
ROWS = NF + SH
ZF = 9
ZT = NF // ZF
ZP = ZF * SH
QB = 4
NG = 7
H1, H2 = 512, 256


def dlrm_kernel(nc, x, ids, tables, w_pairs, w_dense, b1, w2, b2, w3, out):
    fp32, i32 = mybir.dt.float32, mybir.dt.int32
    ALU, ACT = mybir.AluOpType, mybir.ActivationFunctionType

    with ExitStack() as ctx:
        def sb(name, shape, dt=fp32):
            return ctx.enter_context(nc.sbuf_tensor(name, shape, dt))

        def ps(name, shape):
            return ctx.enter_context(nc.psum_tensor(name, shape, fp32))

        def sem(name):
            return ctx.enter_context(nc.semaphore(name))

        idx = sb("idx", [P, T, F], i32)
        rows = sb("rows", [P, T, F, P])
        dense = sb("dense", [P, T, P])
        ET = sb("ET", [P, 2, SLOT, P // SLOT, SLOT])
        xT = sb("xT", [P, 2, P])
        S = sb("S", [P, 2, NF, SLOT])
        G = sb("G", [P, ROWS, SLOT])
        z = sb("z", [P, 2, NF, SH])
        zT = sb("zT", [P, 2, ZT, P])
        h1 = sb("h1", [P, H1])
        h1T = sb("h1T", [P, H1 // P, P])
        h2 = sb("h2", [P, H2])
        h2w = sb("h2w", [P, H2])
        y = sb("y", [P, T])
        wp = sb("wp", [P, ZT, H1])
        wd = sb("wd", [P, 2, H1])
        wds = sb("wds", [P, H1])
        w2s = sb("w2s", [P, H1 // P, H2])
        b2s = sb("b2s", [P, H2])
        w3s = sb("w3s", [P, H2])
        zero = sb("zero", [P, P])
        ident = sb("ident", [P, P])

        TP = [ps(f"TP{i}", [P, QB, P]) for i in range(2)]
        GP = [ps(f"GP{i}", [P, 2, 512]) for i in range(2)]
        PL = ps("PL", [P, H1])
        PM = ps("PM", [P, 512])

        s_ids, s_x, s_wp, s_wd, s_w2, s_bw = (sem(n) for n in ("s_ids", "s_x", "s_wp", "s_wd", "s_w2", "s_bw"))
        s_gath = [[sem(f"s_gath{t}_{n}") for n in range(NG)] for t in range(T)]
        s_zero = sem("s_zero")
        s_ident = sem("s_ident")
        s_fill = sem("s_fill")
        s_wds = sem("s_wds")
        s_tp = [sem("s_tp0"), sem("s_tp1")]
        s_et = [sem("s_et0"), sem("s_et1")]
        s_gram = sem("s_gram")
        s_sa = sem("s_sa")
        s_sv = sem("s_sv")
        s_g = sem("s_g")
        s_pick = sem("s_pick")
        s_z = sem("s_z")
        s_zc = sem("s_zc")
        s_l1 = sem("s_l1")
        s_h1 = sem("s_h1")
        s_ht = sem("s_ht")
        s_htc = sem("s_htc")
        s_l2 = sem("s_l2")
        s_h2 = sem("s_h2")
        s_y = sem("s_y")
        s_out = sem("s_out")
        block = ctx.enter_context(nc.Block())

        def feats(n):
            return range(QB * n, min(QB * n + QB, NF))

        def circular():
            return bass.AP(G[:, :, :].tensor, G[:, :, :].offset + SLOT,
                           [list(G[:, :, :].ap[0]), [SLOT + 1, NF], [SLOT, SH]])

        @block.sync
        def _(sp):
            sp.dma_start(idx[:, :, :], ids.rearrange("(p t) f -> p t f", t=T)).then_inc(s_ids, 16)
            sp.dma_start(dense[:, :, :], x.rearrange("(p t) d -> p t d", t=T)).then_inc(s_x, 16)
            sp.dma_start(wd[:, :, :], w_dense.rearrange("a k n -> k a n")).then_inc(s_wd, 16)
            sp.dma_start(wp[0:ZP, :, :], w_pairs.rearrange("i k n -> k i n")).then_inc(s_wp, 16)
            sp.dma_start(wp[ZP:ZP + 1, ZT - 1, :], b1.rearrange("(a n) -> a n", a=1)).then_inc(s_wp, 16)
            sp.dma_start(w2s[:, :, :], w2.rearrange("(c k) n -> k c n", k=P)).then_inc(s_w2, 16)
            sp.dma_start(b2s[:, :], b2.rearrange("(a n) -> a n", a=1).to_broadcast([P, H2])).then_inc(s_bw, 16)
            sp.dma_start(w3s[:, :], w3.rearrange("n a -> a n").to_broadcast([P, H2])).then_inc(s_bw, 16)
            sp.wait_ge(s_y, T)
            sp.dma_start(out.rearrange("(p t) a -> p (t a)", t=T), y[:, :]).then_inc(s_out, 16)
            sp.wait_ge(s_out, 16)

        @block.gpsimd
        def _(pool):
            nc.gpsimd.memset(zero[:, :], 0.0).then_inc(s_zero, 1)
            pool.wait_ge(s_zero, 1)
            nc.gpsimd.affine_select(out=ident[:, :], in_=zero[:, :], compare_op=ALU.not_equal, fill=1.0,
                                    base=0, pattern=[[-1, P]], channel_multiplier=1).then_inc(s_ident, 1)
            pool.wait_ge(s_ids, 16)
            for t in range(T):
                for f in range(F):
                    pool.indirect_dma_start(
                        out=rows[:, t, f, :], out_offset=None, in_=tables[f],
                        in_offset=bass.IndirectOffsetOnAxis(ap=idx[:, t, f:f + 1], axis=0),
                    ).then_inc(s_gath[t][f // QB], 16)

        def copy_features(eng, copy, t, n):
            i = NG * t + n
            eng.wait_ge(s_tp[i % 2], i // 2 + 1)
            if t >= 2:
                eng.wait_ge(s_l1, t - 1)
            if i < 2:
                eng.wait_ge(s_fill, 1)
            fs = feats(n)
            if fs[-1] == F:
                copy(xT[:, t % 2, :], TP[i % 2][:, len(fs) - 1, :])
            copy(ET[:, t % 2, :, :, fs[0]:fs[-1] + 1].rearrange("d r q f -> d f q r"),
                 TP[i % 2][:, 0:len(fs), :].rearrange("d f (q r) -> d f q r", r=SLOT)).then_inc(s_et[i % 2], 1)

        def copy_products(eng, copy, done, t, quadrants):
            if t >= 2:
                eng.wait_ge(s_g, 2 * (t - 1))
            for m in range(4):
                k = 4 * t + m
                eng.wait_ge(s_gram, k + 1)
                for j in quadrants:
                    q = slice(SLOT * j, SLOT * (j + 1))
                    src = GP[k % 2][q, :, 0:16 * NF].rearrange("p b (r c) -> p b r c", r=4)[:, :, :, NF * j:NF * (j + 1)]
                    dst = S[q, t % 2, :, 8 * m:8 * m + 8].rearrange("p g (b r) -> p b r g", b=2)
                    last = copy(dst, src)
                last.then_inc(done, 1)

        @block.scalar
        def _(act):
            def copy(dst, src):
                return nc.scalar.activation(dst, src, ACT.Copy)

            def pairs(t):
                act.wait_ge(s_z, t + 1)
                if t >= 2:
                    act.wait_ge(s_l1, t - 1)
                copy(zT[0:ZP, t % 2, :, :], PM[0:ZP, 0:ZT * P].rearrange("k (i p) -> k i p", i=ZT)).then_inc(s_zc, 1)

            def relu1(t):
                act.wait_ge(s_l1, t + 1)
                if t >= 1:
                    act.wait_ge(s_ht, t)
                nc.scalar.activation(h1[:, :], PL[:, :], ACT.Relu).then_inc(s_h1, 1)

            for t in range(T + 1):
                for n in range(NG):
                    if t < T and (NG * t + n) % 2 == 0:
                        copy_features(act, copy, t, n)
                    if t >= 1 and n == 1:
                        pairs(t - 1)
                    if t >= 1 and n == 2:
                        relu1(t - 1)
                if t < T:
                    copy_products(act, copy, s_sa, t, (0, 1))

        @block.vector
        def _(dve):
            def copy(dst, src):
                return nc.vector.tensor_copy(dst, src)

            def swap(t):
                dve.wait_ge(s_sa, 4 * (t + 1))
                dve.wait_ge(s_sv, 4 * (t + 1))
                if t >= 1:
                    dve.wait_ge(s_pick, t)
                nc.vector.transpose(G[:, 0:NF, :], S[:, t % 2, :, :]).then_inc(s_g, 1)
                nc.vector.transpose(G[:, NF:ROWS, :], S[:, t % 2, 0:SH, :]).then_inc(s_g, 1)
                dve.wait_ge(s_g, 2 * (t + 1))
                if t >= 2:
                    dve.wait_ge(s_z, t - 1)
                copy(z[:, t % 2, :, :], circular()).then_inc(s_pick, 1)

            def hidden(t):
                dve.wait_ge(s_ht, t + 1)
                if t >= 1:
                    dve.wait_ge(s_l2, t)
                copy(h1T[:, :, :], PM[:, :].rearrange("k (c p) -> k c p", c=H1 // P)).then_inc(s_htc, 1)

            def score(t):
                dve.wait_ge(s_l2, t + 1)
                if t == 0:
                    dve.wait_ge(s_bw, 32)
                if t >= 1:
                    dve.wait_ge(s_y, t)
                nc.vector.tensor_tensor(h2[:, :], PM[:, 0:H2], b2s[:, :], ALU.add).then_inc(s_h2, 1)
                dve.wait_ge(s_h2, t + 1)
                nc.vector.scalar_tensor_tensor(out=h2w[:, :], in0=h2[:, :], scalar=0.0, in1=w3s[:, :],
                                               op0=ALU.max, op1=ALU.mult,
                                               accum_out=y[:, t:t + 1]).then_inc(s_y, 1)

            nc.vector.memset(ET[:, :, :, :, NF:SLOT], 0.0)
            nc.vector.memset(zT[:, :, :, :], 1.0).then_inc(s_fill, 1)
            for t in range(T + 1):
                for n in range(NG):
                    if t < T and (NG * t + n) % 2 == 1:
                        copy_features(dve, copy, t, n)
                    if t == 0 and n == 1:
                        dve.wait_ge(s_wd, 16)
                        nc.vector.tensor_tensor(wds[:, :], wd[:, 0, :], wd[:, 1, :], ALU.add).then_inc(s_wds, 1)
                    if t >= 1 and n == 3:
                        hidden(t - 1)
                    if t >= 1 and n == 4:
                        score(t - 1)
                if t < T:
                    copy_products(dve, copy, s_sv, t, (2, 3))
                    swap(t)

        @block.tensor
        def _(pe):
            def transposes(t, n):
                i = NG * t + n
                fs = feats(n)
                pe.wait_ge(s_gath[t][n], 16 * len([f for f in fs if f < F]))
                if i >= 2:
                    pe.wait_ge(s_et[i % 2], i // 2)
                for k, f in enumerate(fs):
                    src = rows[:, t, f, :] if f < F else dense[:, t, :]
                    last = nc.tensor.transpose(TP[i % 2][:, k, :], src, ident[:, :])
                last.then_inc(s_tp[i % 2], 1)

            def products(t):
                for b in range(2):
                    pe.wait_ge(s_et[b], (NG * (t + 1) + 1 - b) // 2)
                for m in range(4):
                    k = 4 * t + m
                    if k >= 2:
                        pe.wait_ge(s_sa, k - 1)
                        pe.wait_ge(s_sv, k - 1)
                    for r in range(8 * m, 8 * m + 8):
                        four = ET[:, t % 2, r, :, :]
                        c = 4 * NF * (r % 4)
                        last = nc.tensor.matmul(GP[k % 2][:, (r // 4) % 2, c:c + 4 * NF], four, four[:, :, 0:NF],
                                                start=True, stop=True)
                    last.then_inc(s_gram, 1)

            def pair_transposes(t):
                pe.wait_ge(s_pick, t + 1)
                if t >= 1:
                    pe.wait_ge(s_h2, t)
                for i in range(ZT):
                    last = nc.tensor.transpose(PM[0:ZP, P * i:P * (i + 1)], z[:, t % 2, ZF * i:ZF * (i + 1), :], ident[:, :])
                last.then_inc(s_z, 1)

            def layer1(t):
                if t == 0:
                    pe.wait_ge(s_wds, 1)
                    pe.wait_ge(s_wp, 32)
                if t >= 1:
                    pe.wait_ge(s_h1, t)
                nc.tensor.matmul(PL[:, :], xT[:, t % 2, :], wds[:, :], start=True, stop=False)
                pe.wait_ge(s_zc, t + 1)
                for i in range(ZT):
                    k = ZP + (i == ZT - 1)
                    last = nc.tensor.matmul(PL[:, :], zT[0:k, t % 2, i, :], wp[0:k, i, :],
                                            start=False, stop=i == ZT - 1)
                last.then_inc(s_l1, 1)

            def hidden_transposes(t):
                pe.wait_ge(s_h1, t + 1)
                for c in range(H1 // P):
                    last = nc.tensor.transpose(PM[:, P * c:P * (c + 1)], h1[:, P * c:P * (c + 1)], ident[:, :])
                last.then_inc(s_ht, 1)

            def layer2(t):
                if t == 0:
                    pe.wait_ge(s_w2, 16)
                pe.wait_ge(s_htc, t + 1)
                for c in range(H1 // P):
                    last = nc.tensor.matmul(PM[:, 0:H2], h1T[:, c, :], w2s[:, c, :],
                                            start=c == 0, stop=c == H1 // P - 1)
                last.then_inc(s_l2, 1)

            pe.wait_ge(s_ident, 1)
            pe.wait_ge(s_x, 16)
            for t in range(T + 1):
                for n in range(NG):
                    if t < T:
                        transposes(t, n)
                    if t >= 1 and n == 1:
                        pair_transposes(t - 1)
                    if t >= 1 and n == 2:
                        layer1(t - 1)
                    if t >= 1 and n == 3:
                        hidden_transposes(t - 1)
                    if t >= 1 and n == 4:
                        layer2(t - 1)
                if t < T:
                    products(t)


def pair_rows():
    order = []
    for f in range(NF):
        for s in range(1, SH + 1):
            a, b = sorted((f, (f + s) % NF))
            if b == F:
                order.append(P + a)
            else:
                order.append(P + F + a * F - a * (a + 1) // 2 + b - a - 1)
    return order


def kernel(**inputs):
    import numpy as np
    import concourse.bacc as bacc
    from concourse import mybir as mb
    from concourse.bass_utils import run_bass_kernel_spmd

    w1 = np.asarray(inputs["W_top1"])
    arrays = {name: np.ascontiguousarray(a) for name, a in inputs.items() if name != "W_top1"}
    arrays["w_pairs"] = np.ascontiguousarray(w1[pair_rows()].reshape(ZT, ZP, H1))
    arrays["w_dense"] = np.ascontiguousarray(np.stack([w1[0:P], w1[-P:]]))
    nc = bacc.Bacc("TRN2", target_bir_lowering=False, num_devices=1)
    ap = {name: nc.dram_tensor("in_" + name, a.shape, mb.dt.from_np(a.dtype), kind="ExternalInput").ap()
          for name, a in arrays.items()}
    batch = arrays["ids"].shape[0]
    out = nc.dram_tensor("out_0", (batch, 1), mb.dt.float32, kind="ExternalOutput").ap()
    dlrm_kernel(nc, ap["r_dense_features"], ap["ids"], [ap[f"tbl_{f}"] for f in range(F)], ap["w_pairs"],
                ap["w_dense"], ap["b_top1"], ap["W_top2"], ap["b_top2"], ap["W_top3"], out)
    r = run_bass_kernel_spmd(nc, [{"in_" + name: a for name, a in arrays.items()}], core_ids=[0])
    return r.results[0]["out_0"]
```

```python
import concourse.bass as bass
from concourse import mybir
from contextlib import ExitStack

P = 128
F = 26
NF = F + 1
SLOT = 32
T = 4
SH = NF // 2
ROWS = NF + SH
ZF = 9
ZT = NF // ZF
ZP = ZF * SH
QB = 4
TABLE_ROWS = [12500, 1250, 125000, 12500, 1250, 1000, 12500, 1250, 1250, 12500, 12500, 1000, 1000, 1000,
              1250, 12500, 1250, 12500, 12500, 1250, 1000, 1250, 1250, 1250, 1000, 1000]
NP = 9
PICKED = sorted(range(F), key=lambda f: TABLE_ROWS[f])[:NP]
GATHERED = [f for f in range(F) if f not in PICKED]
NGA = len(GATHERED)
SLOTS = GATHERED + [F] + PICKED
OP = 125
CH = [TABLE_ROWS[f] // OP for f in PICKED]
MAXCH = max(CH)
ACT_BLOCKS = 1
WARM = 20
BUF = 3
RING = 12
NG = -(-(NGA + 1) // QB)
H1, H2 = 512, 256


def dlrm_kernel(nc, x, ids, ids_picked, tables, w_pairs, w_dense, b1, w2, b2, w3, out):
    fp32, fp32r, i32 = mybir.dt.float32, mybir.dt.float32r, mybir.dt.int32
    ALU, ACT = mybir.AluOpType, mybir.ActivationFunctionType

    with ExitStack() as ctx:
        def sb(name, shape, dt=fp32):
            return ctx.enter_context(nc.sbuf_tensor(name, shape, dt))

        def ps(name, shape):
            return ctx.enter_context(nc.psum_tensor(name, shape, fp32))

        def sem(name):
            return ctx.enter_context(nc.semaphore(name))

        idx = sb("idx", [P, T, F], i32)
        rows = sb("rows", [P, 2, NGA, P])
        idp = sb("idp", [OP, BUF, T, P], i32)
        key = sb("key", [OP, len(set(CH)), MAXCH])
        keyi = sb("keyi", [OP, len(set(CH)), MAXCH], i32)
        raw = sb("raw", [OP, BUF, MAXCH, P])
        hi = sb("hi", [OP, 2, MAXCH, P], fp32r)
        lo = sb("lo", [OP, 2, MAXCH, P], fp32r)
        dist = sb("dist", [OP, T * P])
        hot = sb("hot", [OP, RING, T * P], fp32r)
        dense = sb("dense", [P, T, P])
        ET = sb("ET", [P, T, SLOT, P // SLOT, SLOT])
        xT = sb("xT", [P, T, P])
        G = sb("G", [P, ROWS, SLOT])
        z = sb("z", [P, 2, NF, SH])
        zT = sb("zT", [P, 2, ZT, P])
        h1T = sb("h1T", [P, H1 // P, P])
        h2 = sb("h2", [P, H2])
        h2w = sb("h2w", [P, H2])
        y = sb("y", [P, T])
        wp = sb("wp", [P, ZT, H1])
        wd = sb("wd", [P, 2, H1])
        wds = sb("wds", [P, H1])
        w2s = sb("w2s", [P, H1 // P, H2])
        b2s = sb("b2s", [P, H2])
        w3s = sb("w3s", [P, H2])
        zero = sb("zero", [P, P])
        ident = sb("ident", [P, P])

        TP = [ps(f"TP{i}", [P, QB, P]) for i in range(2)]
        GP = [ps(f"GP{i}", [P, SLOT, SLOT]) for i in range(2)]
        PL = ps("PL", [P, H1])
        PM = ps("PM", [P, 512])

        s_ids, s_x, s_wp, s_wd, s_w2, s_bw = (sem(n) for n in ("s_ids", "s_x", "s_wp", "s_wd", "s_w2", "s_bw"))
        s_gath = [[sem(f"s_gath{t}_{n}") for n in range(NG)] for t in range(T)]
        s_zero = sem("s_zero")
        s_ident = sem("s_ident")
        s_fill = sem("s_fill")
        s_wds = sem("s_wds")
        s_tp = sem("s_tp")
        s_et = sem("s_et")
        s_key = sem("s_key")
        s_raw = [[sem(f"s_raw{b}"), sem(f"s_idp{b}")] for b in range(BUF)]
        s_hi = sem("s_hi")
        s_lo = sem("s_lo")
        s_hot = [sem("s_hot0"), sem("s_hot1")]
        s_dist = sem("s_dist")
        s_used = sem("s_used")
        s_pc = sem("s_pc")
        s_gram = sem("s_gram")
        s_g = sem("s_g")
        s_zp = sem("s_zp")
        s_z = sem("s_z")
        s_zc = sem("s_zc")
        s_l1 = sem("s_l1")
        s_h1 = sem("s_h1")
        s_l2 = sem("s_l2")
        s_h2 = sem("s_h2")
        s_y = sem("s_y")
        s_out = sem("s_out")
        block = ctx.enter_context(nc.Block())

        PB = [PL, PM]

        def slots(n):
            return range(QB * n, min(QB * n + QB, NGA + 1))

        def used(j):
            return sum(CH[:j])

        def builder(j, c):
            return 0 if c >= CH[j] - ACT_BLOCKS else 1

        def built(e, j, c):
            return sum(len([b for b in range(CH[i]) if builder(i, b) == e and (i < j or b <= c)]) for i in range(j + 1))

        def kind(j):
            return sorted(set(CH)).index(CH[j])

        def banks(t, m):
            first = NG * (t + 1)
            if not 0 <= t < T - 1:
                return range(0)
            ends = [first + 2, first + 4, first + NG, first + NG] if t == 0 else \
                [first + 1, first + 2, first + 3, first + NG]
            return range(max(ends[m - 1] if m else first, NP - 1), ends[m])

        def circular():
            return bass.AP(G[:, :, :].tensor, G[:, :, :].offset + SLOT,
                           [list(G[:, :, :].ap[0]), [SLOT + 1, NF], [SLOT, SH]])

        def load_table(queue, j):
            queue.dma_start(raw[:, j % BUF, 0:CH[j], :],
                            tables[PICKED[j]].rearrange("(p c) d -> p c d", p=OP)).then_inc(s_raw[j % BUF][0], 16)

        def load_ids(queue, j):
            queue.dma_start(idp[:, j % BUF, :, :].rearrange("k t p -> k (t p)"),
                            ids_picked[j:j + 1, :, :].rearrange("a t p -> a (t p)").to_broadcast([OP, T * P])
                            ).then_inc(s_raw[j % BUF][1], 16)

        @block.sync
        def _(sp):
            sp.dma_start(idx[:, :, :], ids.rearrange("(p t) f -> p t f", t=T)).then_inc(s_ids, 16)

            def load_picked(j):
                if j >= BUF:
                    sp.wait_ge(s_lo, j - BUF + 1)
                if j >= 1:
                    load_table(sp, j)
                if j >= BUF:
                    for e in range(2):
                        sp.wait_ge(s_hot[e], built(e, j - BUF, CH[j - BUF] - 1))
                load_ids(sp, j)

            for j in range(BUF + 1):
                load_picked(j)
            sp.dma_start(dense[:, :, :], x.rearrange("(p t) d -> p t d", t=T)).then_inc(s_x, 16)
            sp.dma_start(wd[:, :, :], w_dense.rearrange("a k n -> k a n")).then_inc(s_wd, 16)
            load_picked(BUF + 1)
            sp.dma_start(wp[0:ZP, :, :], w_pairs.rearrange("i k n -> k i n")).then_inc(s_wp, 16)
            sp.dma_start(wp[ZP:ZP + 1, ZT - 1, :], b1.rearrange("(a n) -> a n", a=1)).then_inc(s_wp, 16)
            load_picked(BUF + 2)
            sp.dma_start(w2s[:, :, :], w2.rearrange("(c k) n -> k c n", k=P)).then_inc(s_w2, 16)
            sp.dma_start(b2s[:, :], b2.rearrange("(a n) -> a n", a=1).to_broadcast([P, H2])).then_inc(s_bw, 16)
            sp.dma_start(w3s[:, :], w3.rearrange("n a -> a n").to_broadcast([P, H2])).then_inc(s_bw, 16)
            for j in range(BUF + 3, NP):
                load_picked(j)
            sp.wait_ge(s_y, T)
            sp.dma_start(out.rearrange("(p t) a -> p (t a)", t=T), y[:, :]).then_inc(s_out, 16)
            sp.wait_ge(s_out, 16)

        @block.gpsimd
        def _(pool):
            nc.gpsimd.memset(zero[:, :], 0.0).then_inc(s_zero, 1)
            pool.wait_ge(s_zero, 1)
            nc.gpsimd.affine_select(out=ident[:, :], in_=zero[:, :], compare_op=ALU.not_equal, fill=1.0,
                                    base=0, pattern=[[-1, P]], channel_multiplier=1).then_inc(s_ident, 1)
            for k, ch in enumerate(sorted(set(CH))):
                nc.gpsimd.iota(keyi[:, k, :], pattern=[[1, MAXCH]], base=0, channel_multiplier=ch).then_inc(s_key, 1)
            pool.wait_ge(s_ids, 16)
            for t in range(T):
                for k, f in enumerate(GATHERED):
                    if t >= 2 and k % QB == 0:
                        pool.wait_ge(s_tp, NG * (t - 2) + k // QB + 1)
                    pool.indirect_dma_start(
                        out=rows[:, t % 2, k, :], out_offset=None, in_=tables[f],
                        in_offset=bass.IndirectOffsetOnAxis(ap=idx[:, t, f:f + 1], axis=0),
                    ).then_inc(s_gath[t][k // QB], 16)

        def copy_features(eng, copy, i):
            t, n = i // NG, i % NG
            eng.wait_ge(s_tp, i + 1)
            fs = slots(n)
            if fs[-1] == NGA:
                copy(xT[:, t, :], TP[i % 2][:, len(fs) - 1, :])
            copy(ET[:, t, :, :, fs[0]:fs[-1] + 1].rearrange("d r q f -> d f q r"),
                 TP[i % 2][:, 0:len(fs), :].rearrange("d f (q r) -> d f q r", r=SLOT)).then_inc(s_et, 1)

        @block.scalar
        def _(act):
            def copy(dst, src):
                return nc.scalar.activation(dst, src, ACT.Copy)

            def pairs(t):
                act.wait_ge(s_z, t + 1)
                if t == 0:
                    act.wait_ge(s_fill, 1)
                if t >= 2:
                    act.wait_ge(s_l1, t - 1)
                copy(zT[0:ZP, t % 2, :, :], PM[0:ZP, 0:ZT * P].rearrange("k (i p) -> k i p", i=ZT)).then_inc(s_zc, 1)

            def relu1(t):
                act.wait_ge(s_l1, t + 1)
                if t >= 1:
                    act.wait_ge(s_l2, t)
                nc.scalar.activation(h1T[:, :, :].rearrange("k c p -> k (c p)"), PL[:, :], ACT.Relu).then_inc(s_h1, 1)

            def split_hi(j):
                act.wait_ge(s_raw[j % BUF][0], 16 * (j // BUF + 1))
                if j >= 2:
                    act.wait_ge(s_used, used(j - 1))
                copy(hi[:, j % 2, 0:CH[j], :], raw[:, j % BUF, 0:CH[j], :]).then_inc(s_hi, 1)

            def picked(j):
                act.wait_ge(s_used, used(j + 1))
                copy(ET[:, :, :, :, NGA + 1 + j].rearrange("d t r q -> d t q r"),
                     PB[j % 2][:, :].rearrange("d (t q r) -> d t q r", t=T, r=SLOT)).then_inc(s_pc, 1)

            def one_hot(j):
                act.wait_ge(s_raw[j % BUF][1], 16 * (j // BUF + 1))
                if j == 0:
                    act.wait_ge(s_key, len(set(CH)) + 1)
                for c in range(CH[j]):
                    q = used(j) + c
                    if builder(j, c) != 0:
                        continue
                    b = built(0, j, c)
                    if b > 1:
                        act.wait_ge(s_hot[0], b - 1)
                    nc.scalar.activation(dist[:, :], idp[:, j % BUF, :, :].rearrange("k t p -> k (t p)"), ACT.Abs,
                                         bias=key[:, kind(j), c:c + 1], scale=-1.0).then_inc(s_dist, 1)
                    act.wait_ge(s_dist, b)
                    if q >= RING:
                        act.wait_ge(s_used, q - RING + 1)
                    nc.scalar.activation(hot[:, q % RING, :], dist[:, :], ACT.Relu,
                                         bias=1.0, scale=-1.0).then_inc(s_hot[0], 1)

            load_table(act, 0)
            split_hi(0)
            one_hot(0)
            for j in range(NP):
                if j + 1 < NP:
                    split_hi(j + 1)
                    one_hot(j + 1)
                if j == 0:
                    nc.scalar.memzero(ET[:, :, :, :, NF:SLOT]).then_inc(s_fill, 1)
                picked(j)
                if j >= 1:
                    copy_features(act, copy, j - 1)
            for t in range(T):
                for m in range(4):
                    if t >= 1 and m == 1:
                        pairs(t - 1)
                    if t >= 1 and m == (3 if t == T - 1 else 2):
                        relu1(t - 1)
                    for i in banks(t, m):
                        copy_features(act, copy, i)
            pairs(T - 1)
            relu1(T - 1)

        @block.vector
        def _(dve):
            def copy(dst, src):
                return nc.vector.tensor_copy(dst, src)

            def swap(t):
                dve.wait_ge(s_gram, t + 1)
                by_pair = GP[t % 2][:, :, 0:NF].rearrange("p r g -> p g r")
                if t >= 1:
                    dve.wait_ge(s_zp, t)
                nc.vector.transpose(G[:, 0:NF, :], by_pair).then_inc(s_g, 1)
                nc.vector.transpose(G[:, NF:ROWS, :], by_pair[:, 0:SH, :]).then_inc(s_g, 1)
                dve.wait_ge(s_g, 2 * (t + 1))
                if t >= 2:
                    dve.wait_ge(s_z, t - 1)
                copy(z[:, t % 2, :, :], circular()).then_inc(s_zp, 1)

            def score(t):
                dve.wait_ge(s_l2, t + 1)
                if t == 0:
                    dve.wait_ge(s_bw, 32)
                if t >= 1:
                    dve.wait_ge(s_y, t)
                nc.vector.tensor_tensor(h2[:, :], PM[:, 0:H2], b2s[:, :], ALU.add).then_inc(s_h2, 1)
                dve.wait_ge(s_h2, t + 1)
                nc.vector.scalar_tensor_tensor(out=h2w[:, :], in0=h2[:, :], scalar=0.0, in1=w3s[:, :],
                                               op0=ALU.max, op1=ALU.mult,
                                               accum_out=y[:, t:t + 1]).then_inc(s_y, 1)

            def split_lo(j):
                dve.wait_ge(s_hi, j + 1)
                if j >= 2:
                    dve.wait_ge(s_used, used(j - 1))
                nc.vector.tensor_tensor(lo[:, j % 2, 0:CH[j], :], raw[:, j % BUF, 0:CH[j], :],
                                        hi[:, j % 2, 0:CH[j], :].bitcast(fp32), ALU.subtract).then_inc(s_lo, 1)

            def one_hot(j):
                dve.wait_ge(s_raw[j % BUF][1], 16 * (j // BUF + 1))
                for c in range(CH[j]):
                    q = used(j) + c
                    if builder(j, c) != 1:
                        continue
                    if q >= RING:
                        dve.wait_ge(s_used, q - RING + 1)
                    nc.vector.tensor_scalar(hot[:, q % RING, :], idp[:, j % BUF, :, :].rearrange("k t p -> k (t p)"),
                                            key[:, kind(j), c:c + 1], None, ALU.is_equal).then_inc(s_hot[1], 1)

            nc.vector.memset(zT[:, :, :, :], 1.0).then_inc(s_fill, 1)
            dve.wait_ge(s_key, len(set(CH)))
            copy(key[:, :, :], keyi[:, :, :]).then_inc(s_key, 1)
            dve.wait_ge(s_key, len(set(CH)) + 1)
            for j in range(NP):
                one_hot(j)
                split_lo(j)
            dve.wait_ge(s_wd, 16)
            nc.vector.tensor_tensor(wds[:, :], wd[:, 0, :], wd[:, 1, :], ALU.add).then_inc(s_wds, 1)
            for t in range(T + 1):
                if t < T:
                    swap(t)
                if t >= 1:
                    score(t - 1)

        @block.tensor
        def _(pe):
            def look_up(j):
                if j >= 2:
                    pe.wait_ge(s_pc, j - 1)
                for c in range(CH[j]):
                    if c == 0:
                        pe.wait_ge(s_hi, j + 1)
                    pe.wait_ge(s_hot[builder(j, c)], built(builder(j, c), j, c))
                    nc.tensor.matmul(PB[j % 2][:, :], hi[:, j % 2, c, :], hot[:, (used(j) + c) % RING, :],
                                     start=c == 0, stop=False)
                for c in range(CH[j]):
                    if c == 0:
                        pe.wait_ge(s_lo, j + 1)
                    nc.tensor.matmul(PB[j % 2][:, :], lo[:, j % 2, c, :], hot[:, (used(j) + c) % RING, :],
                                     start=False, stop=c == CH[j] - 1).then_inc(s_used, 1)

            def transposes(i):
                t, n = i // NG, i % NG
                fs = slots(n)
                pe.wait_ge(s_gath[t][n], 16 * len([f for f in fs if f < NGA]))
                if i >= 2:
                    pe.wait_ge(s_et, i - 1)
                if i == NG - 1:
                    pe.wait_ge(s_x, 16)
                for k, f in enumerate(fs):
                    src = rows[:, t % 2, f, :] if f < NGA else dense[:, t, :]
                    last = nc.tensor.transpose(TP[i % 2][:, k, :], src, ident[:, :])
                last.then_inc(s_tp, 1)

            def products(t, m):
                if m == 0:
                    pe.wait_ge(s_et, NG * (t + 1))
                    if t == 0:
                        pe.wait_ge(s_pc, NP)
                        pe.wait_ge(s_fill, 2)
                if m == 0 and t >= 2:
                    pe.wait_ge(s_g, 2 * (t - 1))
                for r in range(8 * m, 8 * m + 8):
                    for q in range(4):
                        last = nc.tensor.matmul(GP[t % 2][SLOT * q:SLOT * (q + 1), r, 0:NF],
                                                ET[:, t, r, q, :], ET[:, t, r, q, 0:NF], start=True, stop=True)
                if m == 3:
                    last.then_inc(s_gram, 1)

            def pair_transposes(t):
                pe.wait_ge(s_zp, t + 1)
                if t >= 1:
                    pe.wait_ge(s_h2, min(t, T - 2))
                for i in range(ZT):
                    last = nc.tensor.transpose(PM[0:ZP, P * i:P * (i + 1)], z[:, t % 2, ZF * i:ZF * (i + 1), :], ident[:, :])
                last.then_inc(s_z, 1)

            def layer1(t):
                if t == 0:
                    pe.wait_ge(s_wds, 1)
                    pe.wait_ge(s_wp, 32)
                if t >= 1:
                    pe.wait_ge(s_h1, t)
                pe.wait_ge(s_zc, t + 1)
                for n in range(0, H1, P):
                    nc.tensor.matmul(PL[:, n:n + P], wds[:, n:n + P], xT[:, t, :], start=True, stop=False)
                    for i in range(ZT):
                        k = ZP + (i == ZT - 1)
                        last = nc.tensor.matmul(PL[:, n:n + P], wp[0:k, i, n:n + P], zT[0:k, t % 2, i, :],
                                                start=False, stop=i == ZT - 1)
                last.then_inc(s_l1, 1)

            def layer2(t):
                if t == 0:
                    pe.wait_ge(s_w2, 16)
                pe.wait_ge(s_zc, t + 2 if t == T - 2 else t + 1)
                if t == T - 1:
                    pe.wait_ge(s_h2, t)
                pe.wait_ge(s_h1, t + 1)
                for c in range(H1 // P):
                    last = nc.tensor.matmul(PM[:, 0:H2], h1T[:, c, :], w2s[:, c, :],
                                            start=c == 0, stop=c == H1 // P - 1)
                last.then_inc(s_l2, 1)

            pe.wait_ge(s_ident, 1)
            for k in range(WARM):
                nc.tensor.transpose(PL[:, 0:P], ident[:, :], ident[:, :])
            for j in range(NP):
                look_up(j)
                if j >= 1:
                    transposes(j - 1)
            for t in range(T):
                for m in range(4):
                    products(t, m)
                    if t >= 1 and m == 1:
                        pair_transposes(t - 1)
                    if t >= 1 and m == (3 if t == T - 1 else 2):
                        layer1(t - 1)
                    if 1 <= t < T - 1 and m == 3:
                        layer2(t - 1)
                    for i in banks(t, m):
                        transposes(i)
            pair_transposes(T - 1)
            layer2(T - 2)
            layer1(T - 1)
            layer2(T - 1)


def pair_rows():
    order = []
    for i in range(NF):
        for s in range(1, SH + 1):
            a, b = sorted((SLOTS[i], SLOTS[(i + s) % NF]))
            if b == F:
                order.append(P + a)
            else:
                order.append(P + F + a * F - a * (a + 1) // 2 + b - a - 1)
    return order


def kernel(**inputs):
    import numpy as np
    import concourse.bacc as bacc
    from concourse import mybir as mb
    from concourse.bass_utils import run_bass_kernel_spmd

    w1 = np.asarray(inputs["W_top1"])
    arrays = {name: np.ascontiguousarray(a) for name, a in inputs.items() if name != "W_top1"}
    arrays["w_pairs"] = np.ascontiguousarray(w1[pair_rows()].reshape(ZT, ZP, H1))
    arrays["w_dense"] = np.ascontiguousarray(np.stack([w1[0:P], w1[-P:]]))
    arrays["ids_picked"] = np.ascontiguousarray(arrays["ids"].reshape(P, T, F)[:, :, PICKED].transpose(2, 1, 0))
    nc = bacc.Bacc("TRN2", target_bir_lowering=False, num_devices=1)
    ap = {name: nc.dram_tensor("in_" + name, a.shape, mb.dt.from_np(a.dtype), kind="ExternalInput").ap()
          for name, a in arrays.items()}
    batch = arrays["ids"].shape[0]
    out = nc.dram_tensor("out_0", (batch, 1), mb.dt.float32, kind="ExternalOutput").ap()
    dlrm_kernel(nc, ap["r_dense_features"], ap["ids"], ap["ids_picked"], [ap[f"tbl_{f}"] for f in range(F)],
                ap["w_pairs"], ap["w_dense"], ap["b_top1"], ap["W_top2"], ap["b_top2"], ap["W_top3"], out)
    r = run_bass_kernel_spmd(nc, [{"in_" + name: a for name, a in arrays.items()}], core_ids=[0])
    return r.results[0]["out_0"]
```

```python
import concourse.bass as bass
from concourse import mybir
from contextlib import ExitStack

P = 128
F = 26
NF = F + 1
SLOT = 32
T = 4
SH = NF // 2
ROWS = NF + SH
ZF = 9
ZT = NF // ZF
ZP = ZF * SH
QB = 4
TABLE_ROWS = [12500, 1250, 125000, 12500, 1250, 1000, 12500, 1250, 1250, 12500, 12500, 1000, 1000, 1000,
              1250, 12500, 1250, 12500, 12500, 1250, 1000, 1250, 1250, 1250, 1000, 1000]
NP = 9
PICKED = sorted(range(F), key=lambda f: TABLE_ROWS[f])[:NP]
GATHERED = [f for f in range(F) if f not in PICKED]
NGA = len(GATHERED)
SLOTS = GATHERED + [F] + PICKED
OP = 125
CH = [TABLE_ROWS[f] // OP for f in PICKED]
MAXCH = max(CH)
ACT_BLOCKS = 1
WARM = 20
BUF = 3
RING = 12
AHEAD = 8
BANKS_DONE = (8, 9, 10, 10,
              11, 12, 13, 15,
              16, 16, 16, 18)
FIRST_PARTS = 1
MORE_PARTS = 2
NG = -(-(NGA + 1) // QB)
H1, H2 = 512, 256


def dlrm_kernel(nc, x, ids, ids_picked, tables, w_pairs, w_dense, b1, w2, b2, w3, out):
    fp32, fp32r, i32 = mybir.dt.float32, mybir.dt.float32r, mybir.dt.int32
    ALU, ACT = mybir.AluOpType, mybir.ActivationFunctionType

    with ExitStack() as ctx:
        def sb(name, shape, dt=fp32):
            return ctx.enter_context(nc.sbuf_tensor(name, shape, dt))

        def ps(name, shape):
            return ctx.enter_context(nc.psum_tensor(name, shape, fp32))

        def sem(name):
            return ctx.enter_context(nc.semaphore(name))

        idx = sb("idx", [P, T, F], i32)
        rows = sb("rows", [P, 2, NGA, P])
        idp = sb("idp", [OP, BUF, T, P], i32)
        key = sb("key", [OP, len(set(CH)), MAXCH])
        keyi = sb("keyi", [OP, len(set(CH)), MAXCH], i32)
        raw = sb("raw", [OP, BUF, MAXCH, P])
        hi = sb("hi", [OP, 2, MAXCH, P], fp32r)
        lo = sb("lo", [OP, 2, MAXCH, P], fp32r)
        dist = sb("dist", [OP, T * P])
        hot = sb("hot", [OP, RING, T * P], fp32r)
        dense = sb("dense", [P, T, P])
        ET = sb("ET", [P, T, SLOT, P // SLOT, SLOT])
        xT = sb("xT", [P, T, P])
        G = sb("G", [P, ROWS, SLOT])
        z = sb("z", [P, 2, NF, SH])
        zT = sb("zT", [P, 2, ZT, P])
        h1T = sb("h1T", [P, 2, H1 // P, P])
        h2 = sb("h2", [P, H2])
        h2w = sb("h2w", [P, H2])
        y = sb("y", [P, T])
        wp = sb("wp", [P, ZT, H1])
        wd = sb("wd", [P, 2, H1])
        wds = sb("wds", [P, H1])
        w2s = sb("w2s", [P, H1 // P, H2])
        b2s = sb("b2s", [P, H2])
        w3s = sb("w3s", [P, H2])
        zero = sb("zero", [P, P])
        ident = sb("ident", [P, P])

        TP = [ps(f"TP{i}", [P, QB, P]) for i in range(2)]
        GP = [ps(f"GP{i}", [P, SLOT, SLOT]) for i in range(2)]
        PL = ps("PL", [P, H1])
        PM = ps("PM", [P, 512])

        s_ids, s_x, s_wp, s_wd, s_w2, s_bw = (sem(n) for n in ("s_ids", "s_x", "s_wp", "s_wd", "s_w2", "s_bw"))
        s_gath = [[sem(f"s_gath{t}_{n}") for n in range(NG)] for t in range(T)]
        s_zero = sem("s_zero")
        s_ident = sem("s_ident")
        s_fill = sem("s_fill")
        s_wds = sem("s_wds")
        s_tp = sem("s_tp")
        s_et = sem("s_et")
        s_key = sem("s_key")
        s_raw = [[sem(f"s_raw{b}"), sem(f"s_idp{b}")] for b in range(BUF)]
        s_hi = sem("s_hi")
        s_lo = sem("s_lo")
        s_hot = [sem("s_hot0"), sem("s_hot1")]
        s_dist = sem("s_dist")
        s_used = sem("s_used")
        s_pc = sem("s_pc")
        s_gram = sem("s_gram")
        s_g = sem("s_g")
        s_zp = sem("s_zp")
        s_z = sem("s_z")
        s_zc = sem("s_zc")
        s_l1 = sem("s_l1")
        s_h1 = sem("s_h1")
        s_l2 = sem("s_l2")
        s_h2 = sem("s_h2")
        s_y = sem("s_y")
        s_out = sem("s_out")
        block = ctx.enter_context(nc.Block())

        PB = [PL, PM]

        def first_layer(t):
            return PL[:, :] if t < T - 1 else TP[0][:, :, :].rearrange("p f q -> p (f q)")

        def second_layer(t):
            return PM[:, 0:H2] if t < T - 1 else TP[1][:, 0:H2 // P, :].rearrange("p f q -> p (f q)")

        def slots(n):
            return range(QB * n, min(QB * n + QB, NGA + 1))

        def used(j):
            return sum(CH[:j])

        def builder(j, c):
            return 0 if c >= CH[j] - ACT_BLOCKS else 1

        def built(e, j, c):
            return sum(len([b for b in range(CH[i]) if builder(i, b) == e and (i < j or b <= c)]) for i in range(j + 1))

        def kind(j):
            return sorted(set(CH)).index(CH[j])

        def banks(t, m):
            ends = [AHEAD] + [max(AHEAD, n) for n in BANKS_DONE]
            return range(ends[4 * t + m], ends[4 * t + m + 1])

        def circular():
            return bass.AP(G[:, :, :].tensor, G[:, :, :].offset + SLOT,
                           [list(G[:, :, :].ap[0]), [SLOT + 1, NF], [SLOT, SH]])

        def load_table(queue, j):
            queue.dma_start(raw[:, j % BUF, 0:CH[j], :],
                            tables[PICKED[j]].rearrange("(p c) d -> p c d", p=OP)).then_inc(s_raw[j % BUF][0], 16)

        def load_ids(queue, j):
            queue.dma_start(idp[:, j % BUF, :, :].rearrange("k t p -> k (t p)"),
                            ids_picked[j:j + 1, :, :].rearrange("a t p -> a (t p)").to_broadcast([OP, T * P])
                            ).then_inc(s_raw[j % BUF][1], 16)

        @block.sync
        def _(sp):
            sp.dma_start(idx[:, :, :], ids.rearrange("(p t) f -> p t f", t=T)).then_inc(s_ids, 16)

            def load_picked(j):
                if j < BUF:
                    load_ids(sp, j)
                    load_table(sp, j)
                else:
                    sp.wait_ge(s_lo, j - BUF + 1)
                    load_table(sp, j)
                    for e in range(2):
                        sp.wait_ge(s_hot[e], built(e, j - BUF, CH[j - BUF] - 1))
                    load_ids(sp, j)

            for j in range(BUF + 1):
                load_picked(j)
            sp.dma_start(dense[:, :, :], x.rearrange("(p t) d -> p t d", t=T)).then_inc(s_x, 16)
            sp.dma_start(wd[:, :, :], w_dense.rearrange("a k n -> k a n")).then_inc(s_wd, 16)
            load_picked(BUF + 1)
            sp.dma_start(wp[0:ZP, :, :], w_pairs.rearrange("i k n -> k i n")).then_inc(s_wp, 16)
            sp.dma_start(wp[ZP:ZP + 1, ZT - 1, :], b1.rearrange("(a n) -> a n", a=1)).then_inc(s_wp, 16)
            load_picked(BUF + 2)
            sp.dma_start(w2s[:, :, :], w2.rearrange("(c k) n -> k c n", k=P)).then_inc(s_w2, 16)
            sp.dma_start(b2s[:, :], b2.rearrange("(a n) -> a n", a=1).to_broadcast([P, H2])).then_inc(s_bw, 16)
            sp.dma_start(w3s[:, :], w3.rearrange("n a -> a n").to_broadcast([P, H2])).then_inc(s_bw, 16)
            for j in range(BUF + 3, NP):
                load_picked(j)
            sp.wait_ge(s_y, T)
            sp.dma_start(out.rearrange("(p t) a -> p (t a)", t=T), y[:, :]).then_inc(s_out, 16)
            sp.wait_ge(s_out, 16)

        @block.gpsimd
        def _(pool):
            nc.gpsimd.memset(zero[:, :], 0.0).then_inc(s_zero, 1)
            pool.wait_ge(s_zero, 1)
            nc.gpsimd.affine_select(out=ident[:, :], in_=zero[:, :], compare_op=ALU.not_equal, fill=1.0,
                                    base=0, pattern=[[-1, P]], channel_multiplier=1).then_inc(s_ident, 1)
            for k, ch in enumerate(sorted(set(CH))):
                nc.gpsimd.iota(keyi[:, k, :], pattern=[[1, MAXCH]], base=0, channel_multiplier=ch).then_inc(s_key, 1)
            pool.wait_ge(s_ids, 16)
            for t in range(T):
                for k, f in enumerate(GATHERED):
                    if t >= 2 and k % QB == 0:
                        pool.wait_ge(s_tp, NG * (t - 2) + k // QB + 1)
                    pool.indirect_dma_start(
                        out=rows[:, t % 2, k, :], out_offset=None, in_=tables[f],
                        in_offset=bass.IndirectOffsetOnAxis(ap=idx[:, t, f:f + 1], axis=0),
                    ).then_inc(s_gath[t][k // QB], 16)

        def copy_features(eng, copy, i):
            t, n = i // NG, i % NG
            eng.wait_ge(s_tp, i + 1)
            fs = slots(n)
            if fs[-1] == NGA:
                copy(xT[:, t, :], TP[i % 2][:, len(fs) - 1, :])
            copy(ET[:, t, :, :, fs[0]:fs[-1] + 1].rearrange("d r q f -> d f q r"),
                 TP[i % 2][:, 0:len(fs), :].rearrange("d f (q r) -> d f q r", r=SLOT)).then_inc(s_et, 1)

        @block.scalar
        def _(act):
            def copy(dst, src):
                return nc.scalar.activation(dst, src, ACT.Copy)

            def pairs(t):
                act.wait_ge(s_z, t + 1)
                if t == 0:
                    act.wait_ge(s_fill, 1)
                if t >= 2:
                    act.wait_ge(s_l1, t - 1)
                copy(zT[0:ZP, t % 2, :, :], PM[0:ZP, 0:ZT * P].rearrange("k (i p) -> k i p", i=ZT)).then_inc(s_zc, 1)

            def relu1(t):
                act.wait_ge(s_l1, t + 1)
                if t >= 2:
                    act.wait_ge(s_l2, t - 1)
                nc.scalar.activation(h1T[:, t % 2, :, :].rearrange("k c p -> k (c p)"), first_layer(t),
                                     ACT.Relu).then_inc(s_h1, 1)

            def split_hi(j):
                act.wait_ge(s_raw[j % BUF][0], 16 * (j // BUF + 1))
                if j >= 2:
                    act.wait_ge(s_used, used(j - 1))
                copy(hi[:, j % 2, 0:CH[j], :], raw[:, j % BUF, 0:CH[j], :]).then_inc(s_hi, 1)

            def picked(j):
                act.wait_ge(s_used, used(j + 1))
                copy(ET[:, :, :, :, NGA + 1 + j].rearrange("d t r q -> d t q r"),
                     PB[j % 2][:, :].rearrange("d (t q r) -> d t q r", t=T, r=SLOT)).then_inc(s_pc, 1)

            def one_hot(j):
                act.wait_ge(s_raw[j % BUF][1], 16 * (j // BUF + 1))
                if j == 0:
                    act.wait_ge(s_key, len(set(CH)) + 1)
                for c in range(CH[j]):
                    q = used(j) + c
                    if builder(j, c) != 0:
                        continue
                    b = built(0, j, c)
                    if b > 1:
                        act.wait_ge(s_hot[0], b - 1)
                    nc.scalar.activation(dist[:, :], idp[:, j % BUF, :, :].rearrange("k t p -> k (t p)"), ACT.Abs,
                                         bias=key[:, kind(j), c:c + 1], scale=-1.0).then_inc(s_dist, 1)
                    act.wait_ge(s_dist, b)
                    if q >= RING:
                        act.wait_ge(s_used, q - RING + 1)
                    nc.scalar.activation(hot[:, q % RING, :], dist[:, :], ACT.Relu,
                                         bias=1.0, scale=-1.0).then_inc(s_hot[0], 1)

            split_hi(0)
            one_hot(0)
            for j in range(NP):
                if j + 1 < NP:
                    split_hi(j + 1)
                    one_hot(j + 1)
                if j == 0:
                    nc.scalar.memzero(ET[:, :, :, :, NF:SLOT]).then_inc(s_fill, 1)
                picked(j)
                for i in range(max(j - 1, 0), j if j < NP - 1 else AHEAD):
                    copy_features(act, copy, i)
            for t in range(T - 1):
                for m in range(4):
                    if t >= 1 and m == 1:
                        pairs(t - 1)
                    if t >= 1 and m == (2 if t < T - 2 else 3):
                        relu1(t - 1)
                    if t == T - 2 and m == 3:
                        pairs(t)
                    for i in banks(t, m):
                        copy_features(act, copy, i)
            for i in range(BANKS_DONE[-1], NG * T):
                copy_features(act, copy, i)
            relu1(T - 2)
            pairs(T - 1)
            relu1(T - 1)

        @block.vector
        def _(dve):
            def copy(dst, src):
                return nc.vector.tensor_copy(dst, src)

            def swap(t):
                dve.wait_ge(s_gram, t + 1)
                by_pair = GP[t % 2][:, :, 0:NF].rearrange("p r g -> p g r")
                if t >= 1:
                    dve.wait_ge(s_zp, t)
                nc.vector.transpose(G[:, 0:NF, :], by_pair).then_inc(s_g, 1)
                nc.vector.transpose(G[:, NF:ROWS, :], by_pair[:, 0:SH, :]).then_inc(s_g, 1)
                dve.wait_ge(s_g, 2 * (t + 1))
                if t >= 2:
                    dve.wait_ge(s_z, t - 1)
                copy(z[:, t % 2, :, :], circular()).then_inc(s_zp, 1)

            def score(t):
                dve.wait_ge(s_l2, t + 1)
                if t == 0:
                    dve.wait_ge(s_bw, 32)
                if t >= 1:
                    dve.wait_ge(s_y, t)
                nc.vector.tensor_tensor(h2[:, :], second_layer(t), b2s[:, :], ALU.add).then_inc(s_h2, 1)
                dve.wait_ge(s_h2, t + 1)
                nc.vector.scalar_tensor_tensor(out=h2w[:, :], in0=h2[:, :], scalar=0.0, in1=w3s[:, :],
                                               op0=ALU.max, op1=ALU.mult,
                                               accum_out=y[:, t:t + 1]).then_inc(s_y, 1)

            def split_lo(j):
                dve.wait_ge(s_hi, j + 1)
                if j >= 2:
                    dve.wait_ge(s_used, used(j - 1))
                nc.vector.tensor_tensor(lo[:, j % 2, 0:CH[j], :], raw[:, j % BUF, 0:CH[j], :],
                                        hi[:, j % 2, 0:CH[j], :].bitcast(fp32), ALU.subtract).then_inc(s_lo, 1)

            def one_hot(j):
                dve.wait_ge(s_raw[j % BUF][1], 16 * (j // BUF + 1))
                for c in range(CH[j]):
                    q = used(j) + c
                    if builder(j, c) != 1:
                        continue
                    if q >= RING:
                        dve.wait_ge(s_used, q - RING + 1)
                    nc.vector.tensor_scalar(hot[:, q % RING, :], idp[:, j % BUF, :, :].rearrange("k t p -> k (t p)"),
                                            key[:, kind(j), c:c + 1], None, ALU.is_equal).then_inc(s_hot[1], 1)

            nc.vector.memset(zT[:, :, :, :], 1.0).then_inc(s_fill, 1)
            dve.wait_ge(s_key, len(set(CH)))
            copy(key[:, :, :], keyi[:, :, :]).then_inc(s_key, 1)
            dve.wait_ge(s_key, len(set(CH)) + 1)
            for j in range(NP):
                one_hot(j)
                split_lo(j)
            dve.wait_ge(s_wd, 16)
            nc.vector.tensor_tensor(wds[:, :], wd[:, 0, :], wd[:, 1, :], ALU.add).then_inc(s_wds, 1)
            for t in range(T + 1):
                if t < T:
                    swap(t)
                if t >= 1:
                    score(t - 1)

        @block.tensor
        def _(pe):
            def look_up(j):
                if j >= 2:
                    pe.wait_ge(s_pc, j - 1)
                pe.wait_ge(s_hi, j + 1)
                for c in range(CH[j]):
                    pe.wait_ge(s_hot[builder(j, c)], built(builder(j, c), j, c))
                    nc.tensor.matmul(PB[j % 2][:, :], hi[:, j % 2, c, :], hot[:, (used(j) + c) % RING, :],
                                     start=c == 0, stop=False)
                pe.wait_ge(s_lo, j + 1)
                for c in range(CH[j]):
                    nc.tensor.matmul(PB[j % 2][:, :], lo[:, j % 2, c, :], hot[:, (used(j) + c) % RING, :],
                                     start=False, stop=c == CH[j] - 1).then_inc(s_used, 1)

            def transposes(i):
                t, n = i // NG, i % NG
                fs = slots(n)
                pe.wait_ge(s_gath[t][n], 16 * len([f for f in fs if f < NGA]))
                if i >= 2:
                    pe.wait_ge(s_et, i - 1)
                if i == NG - 1:
                    pe.wait_ge(s_x, 16)
                for k, f in enumerate(fs):
                    src = rows[:, t % 2, f, :] if f < NGA else dense[:, t, :]
                    last = nc.tensor.transpose(TP[i % 2][:, k, :], src, ident[:, :])
                last.then_inc(s_tp, 1)

            def products(t, m):
                if m == 0:
                    pe.wait_ge(s_et, NG * (t + 1))
                    if t == 0:
                        pe.wait_ge(s_pc, NP)
                        pe.wait_ge(s_fill, 2)
                    if t >= 2:
                        pe.wait_ge(s_g, 2 * (t - 1))
                for r in range(8 * m, 8 * m + 8):
                    for q in range(4):
                        last = nc.tensor.matmul(GP[t % 2][SLOT * q:SLOT * (q + 1), r, 0:NF],
                                                ET[:, t, r, q, :], ET[:, t, r, q, 0:NF], start=True, stop=True)
                if m == 3:
                    last.then_inc(s_gram, 1)

            def pair_transposes(t):
                pe.wait_ge(s_zp, t + 1)
                if t >= 1:
                    pe.wait_ge(s_h2, max(1, t - 1))
                for i in range(ZT):
                    last = nc.tensor.transpose(PM[0:ZP, P * i:P * (i + 1)], z[:, t % 2, ZF * i:ZF * (i + 1), :], ident[:, :])
                last.then_inc(s_z, 1)

            def layer1(t, parts=range(H1 // P)):
                if t == 0:
                    pe.wait_ge(s_wds, 1)
                    pe.wait_ge(s_wp, 32)
                if 1 <= t < T - 1:
                    pe.wait_ge(s_h1, t)
                for part in parts:
                    n = P * part
                    nc.tensor.matmul(first_layer(t)[:, n:n + P], wds[:, n:n + P], xT[:, t, :], start=True, stop=False)
                    if part == 0:
                        pe.wait_ge(s_zc, t + 1)
                    for i in range(ZT):
                        k = ZP + (i == ZT - 1)
                        last = nc.tensor.matmul(first_layer(t)[:, n:n + P], wp[0:k, i, n:n + P], zT[0:k, t % 2, i, :],
                                                start=False, stop=i == ZT - 1)
                    if part == H1 // P - 1:
                        last.then_inc(s_l1, 1)

            def layer2(t):
                if t == 0:
                    pe.wait_ge(s_w2, 16)
                if t < T - 1:
                    pe.wait_ge(s_zc, t + 1 if t < T - 3 else t + 2)
                pe.wait_ge(s_h1, t + 1)
                for c in range(H1 // P):
                    last = nc.tensor.matmul(second_layer(t), h1T[:, t % 2, c, :], w2s[:, c, :],
                                            start=c == 0, stop=c == H1 // P - 1)
                last.then_inc(s_l2, 1)

            pe.wait_ge(s_ident, 1)
            for k in range(WARM):
                nc.tensor.transpose(PL[:, 0:P], ident[:, :], ident[:, :])
            for j in range(NP):
                look_up(j)
                for i in range(max(j - 1, 0), j if j < NP - 1 else AHEAD):
                    transposes(i)
            for t in range(T - 1):
                for m in range(4):
                    products(t, m)
                    if t >= 1 and m == 1:
                        pair_transposes(t - 1)
                    if t >= 1 and m == (2 if t < T - 2 else 3):
                        layer1(t - 1)
                    if t == T - 2 and m == 3:
                        pair_transposes(t)
                    for i in banks(t, m):
                        transposes(i)
                if t >= 1:
                    layer2(t - 1)
            layer1(T - 2, range(FIRST_PARTS))
            for i in range(BANKS_DONE[-1], NG * T):
                transposes(i)
            layer1(T - 2, range(FIRST_PARTS, MORE_PARTS))
            for m in range(4):
                products(T - 1, m)
            layer1(T - 2, range(MORE_PARTS, H1 // P))
            pair_transposes(T - 1)
            layer1(T - 1)
            layer2(T - 2)
            layer2(T - 1)


def pair_rows():
    order = []
    for i in range(NF):
        for s in range(1, SH + 1):
            a, b = sorted((SLOTS[i], SLOTS[(i + s) % NF]))
            if b == F:
                order.append(P + a)
            else:
                order.append(P + F + a * F - a * (a + 1) // 2 + b - a - 1)
    return order


def kernel(**inputs):
    import numpy as np
    import concourse.bacc as bacc
    from concourse import mybir as mb
    from concourse.bass_utils import run_bass_kernel_spmd

    w1 = np.asarray(inputs["W_top1"])
    arrays = {name: np.ascontiguousarray(a) for name, a in inputs.items() if name != "W_top1"}
    arrays["w_pairs"] = np.ascontiguousarray(w1[pair_rows()].reshape(ZT, ZP, H1))
    arrays["w_dense"] = np.ascontiguousarray(np.stack([w1[0:P], w1[-P:]]))
    arrays["ids_picked"] = np.ascontiguousarray(arrays["ids"].reshape(P, T, F)[:, :, PICKED].transpose(2, 1, 0))
    nc = bacc.Bacc("TRN2", target_bir_lowering=False, num_devices=1)
    ap = {name: nc.dram_tensor("in_" + name, a.shape, mb.dt.from_np(a.dtype), kind="ExternalInput").ap()
          for name, a in arrays.items()}
    batch = arrays["ids"].shape[0]
    out = nc.dram_tensor("out_0", (batch, 1), mb.dt.float32, kind="ExternalOutput").ap()
    dlrm_kernel(nc, ap["r_dense_features"], ap["ids"], ap["ids_picked"], [ap[f"tbl_{f}"] for f in range(F)],
                ap["w_pairs"], ap["w_dense"], ap["b_top1"], ap["W_top2"], ap["b_top2"], ap["W_top3"], out)
    r = run_bass_kernel_spmd(nc, [{"in_" + name: a for name, a in arrays.items()}], core_ids=[0])
    return r.results[0]["out_0"]
```
